# Optimizing a Trainium2 kernel written in Bass

```python
import numpy as np
import jax
import jax.numpy as jnp

def _softmax(x, axis=-1):
    return jax.nn.softmax(x, axis=axis)

def _gelu(x):
    return jax.nn.gelu(x, approximate=True)

def _silu(x):
    return jax.nn.silu(x)

def _sigmoid(x):
    return jax.nn.sigmoid(x)

def _layernorm(x, axis=-1, eps=1e-05):
    m = jnp.mean(x, axis=axis, keepdims=True)
    v = jnp.var(x, axis=axis, keepdims=True)
    return (x - m) / jnp.sqrt(v + eps)

def _scatter_add(tgt, idx, src, axis=0):
    return tgt.at[idx].add(src)

def _segment_sum(src, seg, n):
    return jax.ops.segment_sum(src, seg, n)
kernel_name = 'mk_gnn_resnorm_d4_gnn_r8_ea9a6d'

def setup_inputs(seed: int=0):
    np.random.seed(seed)
    _w = jnp.asarray

    def _rec_inputs():
        import jax
        import jax.numpy as jnp
        _gk = jax.random.key(seed)
        x = -0.0003713 + 1 * jax.random.normal(jax.random.fold_in(_gk, 1), (12500, 128), jnp.float32)
        src = jax.random.randint(jax.random.fold_in(_gk, 2), (200000,), 0, 12500, jnp.int32)
        dst = jax.random.randint(jax.random.fold_in(_gk, 3), (200000,), 0, 12500, jnp.int32)
        _o = jnp.argsort(dst, stable=True)
        src = src[_o]
        dst = dst[_o]
        edge_attr_50 = 0.000229061 + 1.00009 * jax.random.normal(jax.random.fold_in(_gk, 11), (200000, 50), jnp.float32)
        edge_weight = jax.random.uniform(jax.random.fold_in(_gk, 13), (200000,), jnp.float32, 0.0, 9.99998)
        return (x, src, dst, edge_attr_50, edge_weight)
    x, src, dst, edge_attr_50, edge_weight = _rec_inputs()

    def _L0_gnn_setup():
        import jax, jax.numpy as jnp
        import numpy as np
        N_NODES = 12500
        N_EDGES = 200000
        F_IN = 128
        HEADS = 4
        C_OUT = 32
        NEG_SLOPE = 0.2

        def _gat_forward(x, edge_index, W, att_src, att_dst, bias):
            N = x.shape[0]
            H, C = att_src.shape
            h = (x @ W).reshape(N, H, C)
            loops = jnp.arange(N, dtype=edge_index.dtype)
            src = jnp.concatenate([edge_index[0], loops])
            dst = jnp.concatenate([edge_index[1], loops])
            a_src = jnp.einsum('nhc,hc->nh', h, att_src)
            a_dst = jnp.einsum('nhc,hc->nh', h, att_dst)
            e = jax.nn.leaky_relu(a_src[src] + a_dst[dst], NEG_SLOPE)
            m = jax.ops.segment_max(e, dst, num_segments=N)
            e = jnp.exp(e - m[dst])
            s = jax.ops.segment_sum(e, dst, num_segments=N)
            alpha = e / (s[dst] + 1e-16)
            msg = h[src] * alpha[:, :, None]
            out = jax.ops.segment_sum(msg, dst, num_segments=N).reshape(N, H * C)
            return jnp.tanh(out + bias)
        key = jax.random.key(seed)
        k1, k2, k3, k4, k5, k6 = jax.random.split(key, 6)
        x = jax.random.normal(k1, (N_NODES, F_IN), dtype=jnp.float32)
        edge_index = jax.random.randint(k2, (2, N_EDGES), 0, N_NODES, dtype=jnp.int64)
        W = jax.random.normal(k3, (F_IN, HEADS * C_OUT), dtype=jnp.float32) * (1.0 / np.sqrt(F_IN))
        att_src = jax.random.normal(k4, (HEADS, C_OUT), dtype=jnp.float32) * (1.0 / np.sqrt(C_OUT))
        att_dst = jax.random.normal(k5, (HEADS, C_OUT), dtype=jnp.float32) * (1.0 / np.sqrt(C_OUT))
        bias = jnp.zeros((HEADS * C_OUT,), dtype=jnp.float32)
        return {'x': x, 'edge_index': edge_index, 'W': W, 'att_src': att_src, 'att_dst': att_dst, 'bias': bias}
    _L0_gnn_all = _L0_gnn_setup()
    _L0_gnn_in = {k: v for k, v in _L0_gnn_all.items() if k in ('W', 'att_src', 'att_dst', 'bias')}
    del _L0_gnn_all

    def _L1_gnn_setup():
        import jax, jax.numpy as jnp
        import numpy as np
        N = 6250
        E = 75000
        HID = 128
        NF = 128
        NG = 50
        CUTOFF = 10.0
        LOG2 = float(np.log(2.0))

        def ssp(x):
            return jax.nn.softplus(x) - LOG2
        key = jax.random.key(seed)
        ks = jax.random.split(key, 12)
        h = jax.random.normal(ks[0], (N, HID), dtype=jnp.float32)
        edge_index = jax.random.randint(ks[1], (2, E), 0, N)
        edge_weight = jax.random.uniform(ks[2], (E,), dtype=jnp.float32) * CUTOFF
        edge_attr = jax.random.normal(ks[3], (E, NG), dtype=jnp.float32)

        def xavier(k, shape):
            fan_out, fan_in = shape
            lim = np.sqrt(6.0 / (fan_in + fan_out))
            return jax.random.uniform(k, shape, jnp.float32, -lim, lim)
        mlp_w0 = xavier(ks[4], (NF, NG))
        mlp_b0 = jnp.zeros((NF,), jnp.float32)
        mlp_w2 = xavier(ks[5], (NF, NF))
        mlp_b2 = jnp.zeros((NF,), jnp.float32)
        lin1_w = xavier(ks[6], (NF, HID))
        lin2_w = xavier(ks[7], (HID, NF))
        lin2_b = jnp.zeros((HID,), jnp.float32)
        lin_w = xavier(ks[8], (HID, HID))
        lin_b = jnp.zeros((HID,), jnp.float32)
        return {'h': h, 'edge_index': edge_index, 'edge_weight': edge_weight, 'edge_attr': edge_attr, 'mlp_w0': mlp_w0, 'mlp_b0': mlp_b0, 'mlp_w2': mlp_w2, 'mlp_b2': mlp_b2, 'lin1_w': lin1_w, 'lin2_w': lin2_w, 'lin2_b': lin2_b, 'lin_w': lin_w, 'lin_b': lin_b}
    _L1_gnn_all = _L1_gnn_setup()
    _L1_gnn_in = {k: v for k, v in _L1_gnn_all.items() if k in ('mlp_w0', 'mlp_b0', 'mlp_w2', 'mlp_b2', 'lin1_w', 'lin2_w', 'lin2_b', 'lin_w', 'lin_b')}
    del _L1_gnn_all

    def _L2_gnn_setup():
        import jax, jax.numpy as jnp
        import numpy as np
        N_NODES = 6250
        N_EDGES = 100000
        D_IN = 128
        N_HEAD = 4
        D_OUT = D_IN // N_HEAD
        key = jax.random.key(seed)
        k1, k2, k3, k4, k5 = jax.random.split(key, 5)
        in_feat = jax.random.normal(k1, (N_NODES, D_IN), dtype=jnp.float32)
        edge_ind = jax.random.randint(k2, (2, N_EDGES), 0, N_NODES, dtype=jnp.int64)
        W_proj = jax.random.normal(k3, (D_IN, N_HEAD * D_OUT), dtype=jnp.float32) * (1.0 / np.sqrt(D_IN))
        a_src = jax.random.normal(k4, (1, N_HEAD, D_OUT), dtype=jnp.float32) * (1.0 / np.sqrt(D_OUT))
        a_tgt = jax.random.normal(k5, (1, N_HEAD, D_OUT), dtype=jnp.float32) * (1.0 / np.sqrt(D_OUT))
        bias = jnp.zeros((N_HEAD * D_OUT,), dtype=jnp.float32)
        return {'in_feat': in_feat, 'edge_ind': edge_ind, 'edge_len': N_EDGES, 'W_proj': W_proj, 'a_src': a_src, 'a_tgt': a_tgt, 'bias': bias}
    _L2_gnn_all = _L2_gnn_setup()
    _L2_gnn_in = {k: v for k, v in _L2_gnn_all.items() if k in ('W_proj', 'a_src', 'a_tgt', 'bias')}
    del _L2_gnn_all

    def _L3_gnn_setup():
        import jax, jax.numpy as jnp
        import numpy as np
        N = 12500
        E = 200000
        D_IN, D_PROJ, D_HID = (128, 128, 64)

        def gcn_layer(x, W, b, src, dst, deg, inv_sqrt_deg):
            h = x @ W
            norm = inv_sqrt_deg[src] * inv_sqrt_deg[dst]
            agg = jax.ops.segment_sum(h[src] * norm[:, None], dst, num_segments=x.shape[0])
            agg = agg + h * (1.0 / deg)[:, None]
            return agg + b
        key = jax.random.key(seed)
        ks = jax.random.split(key, 10)
        glorot = lambda k, i, o: jax.random.normal(k, (i, o), jnp.float32) * jnp.sqrt(2.0 / (i + o))
        x = jax.random.normal(ks[0], (N, D_IN), jnp.float32)
        edge_index = jax.random.randint(ks[1], (2, E), 0, N, dtype=jnp.int32)
        W1, b1 = (glorot(ks[2], D_IN, D_PROJ), jnp.zeros((D_PROJ,), jnp.float32))
        W2, b2 = (glorot(ks[3], D_PROJ, D_HID), jnp.zeros((D_HID,), jnp.float32))
        W3, b3 = (glorot(ks[4], D_HID, D_PROJ), jnp.zeros((D_PROJ,), jnp.float32))
        W4, b4 = (glorot(ks[5], D_PROJ, D_IN), jnp.zeros((D_IN,), jnp.float32))
        return dict(x=x, W1=W1, b1=b1, W2=W2, b2=b2, W3=W3, b3=b3, W4=W4, b4=b4, edge_index=edge_index)
    _L3_gnn_all = _L3_gnn_setup()
    _L3_gnn_in = {k: v for k, v in _L3_gnn_all.items() if k in ('W1', 'b1', 'W2', 'b2', 'W3', 'b3', 'W4', 'b4')}
    del _L3_gnn_all
    return {'x': x, 'src': src, 'dst': dst, 'edge_attr_50': edge_attr_50, 'edge_weight': edge_weight, 'L0_gnn_W': _L0_gnn_in['W'], 'L0_gnn_att_src': _L0_gnn_in['att_src'], 'L0_gnn_att_dst': _L0_gnn_in['att_dst'], 'L0_gnn_bias': _L0_gnn_in['bias'], 'L1_gnn_mlp_w0': _L1_gnn_in['mlp_w0'], 'L1_gnn_mlp_b0': _L1_gnn_in['mlp_b0'], 'L1_gnn_mlp_w2': _L1_gnn_in['mlp_w2'], 'L1_gnn_mlp_b2': _L1_gnn_in['mlp_b2'], 'L1_gnn_lin1_w': _L1_gnn_in['lin1_w'], 'L1_gnn_lin2_w': _L1_gnn_in['lin2_w'], 'L1_gnn_lin2_b': _L1_gnn_in['lin2_b'], 'L1_gnn_lin_w': _L1_gnn_in['lin_w'], 'L1_gnn_lin_b': _L1_gnn_in['lin_b'], 'L2_gnn_W_proj': _L2_gnn_in['W_proj'], 'L2_gnn_a_src': _L2_gnn_in['a_src'], 'L2_gnn_a_tgt': _L2_gnn_in['a_tgt'], 'L2_gnn_bias': _L2_gnn_in['bias'], 'L3_gnn_W1': _L3_gnn_in['W1'], 'L3_gnn_b1': _L3_gnn_in['b1'], 'L3_gnn_W2': _L3_gnn_in['W2'], 'L3_gnn_b2': _L3_gnn_in['b2'], 'L3_gnn_W3': _L3_gnn_in['W3'], 'L3_gnn_b3': _L3_gnn_in['b3'], 'L3_gnn_W4': _L3_gnn_in['W4'], 'L3_gnn_b4': _L3_gnn_in['b4']}

def reference(x, src, dst, edge_attr_50, edge_weight, L0_gnn_W, L0_gnn_att_src, L0_gnn_att_dst, L0_gnn_bias, L1_gnn_mlp_w0, L1_gnn_mlp_b0, L1_gnn_mlp_w2, L1_gnn_mlp_b2, L1_gnn_lin1_w, L1_gnn_lin2_w, L1_gnn_lin2_b, L1_gnn_lin_w, L1_gnn_lin_b, L2_gnn_W_proj, L2_gnn_a_src, L2_gnn_a_tgt, L2_gnn_bias, L3_gnn_W1, L3_gnn_b1, L3_gnn_W2, L3_gnn_b2, L3_gnn_W3, L3_gnn_b3, L3_gnn_W4, L3_gnn_b4):
    import jax
    import jax.numpy as jnp

    def _L0_gnn_ref(x, edge_index, W, att_src, att_dst, bias):
        import jax, jax.numpy as jnp
        import numpy as np
        N_NODES = 12500
        N_EDGES = 200000
        F_IN = 128
        HEADS = 4
        C_OUT = 32
        NEG_SLOPE = 0.2

        def _gat_forward(x, edge_index, W, att_src, att_dst, bias):
            N = x.shape[0]
            H, C = att_src.shape
            h = (x @ W).reshape(N, H, C)
            loops = jnp.arange(N, dtype=edge_index.dtype)
            src = jnp.concatenate([edge_index[0], loops])
            dst = jnp.concatenate([edge_index[1], loops])
            a_src = jnp.einsum('nhc,hc->nh', h, att_src)
            a_dst = jnp.einsum('nhc,hc->nh', h, att_dst)
            e = jax.nn.leaky_relu(a_src[src] + a_dst[dst], NEG_SLOPE)
            m = jax.ops.segment_max(e, dst, num_segments=N)
            e = jnp.exp(e - m[dst])
            s = jax.ops.segment_sum(e, dst, num_segments=N)
            alpha = e / (s[dst] + 1e-16)
            msg = h[src] * alpha[:, :, None]
            out = jax.ops.segment_sum(msg, dst, num_segments=N).reshape(N, H * C)
            return jnp.tanh(out + bias)
        return _gat_forward(x, edge_index, W, att_src, att_dst, bias)

    def _L1_gnn_ref(h, edge_index, edge_weight, edge_attr, mlp_w0, mlp_b0, mlp_w2, mlp_b2, lin1_w, lin2_w, lin2_b, lin_w, lin_b):
        import jax, jax.numpy as jnp
        import numpy as np
        N = 6250
        E = 75000
        HID = 128
        NF = 128
        NG = 50
        CUTOFF = 10.0
        LOG2 = float(np.log(2.0))

        def ssp(x):
            return jax.nn.softplus(x) - LOG2
        src, dst = (edge_index[0], edge_index[1])
        h1 = h @ lin1_w.T
        c = 0.5 * (jnp.cos(edge_weight / CUTOFF * jnp.pi) + 1.0)
        W = ssp(edge_attr @ mlp_w0.T + mlp_b0) @ mlp_w2.T + mlp_b2
        message = c[:, None] * (W * h1[src])
        agg = jax.ops.segment_sum(message, dst, num_segments=h.shape[0])
        h2 = (h1 + agg) @ lin2_w.T + lin2_b
        return ssp(h2) @ lin_w.T + lin_b

    def _L2_gnn_ref(in_feat, edge_ind, edge_len, W_proj, a_src, a_tgt, bias):
        import jax, jax.numpy as jnp
        import numpy as np
        N_NODES = 6250
        N_EDGES = 100000
        D_IN = 128
        N_HEAD = 4
        D_OUT = D_IN // N_HEAD
        n_nodes = in_feat.shape[0]
        n_head, d_out = (a_src.shape[1], a_src.shape[2])
        proj_feat = (in_feat @ W_proj).reshape(n_nodes, n_head, d_out)
        src_score = jnp.sum(proj_feat * a_src, axis=-1)
        tgt_score = jnp.sum(proj_feat * a_tgt, axis=-1)
        src_ind, tgt_ind = (edge_ind[0], edge_ind[1])
        edge_score = jax.nn.leaky_relu(src_score[src_ind] + tgt_score[tgt_ind], negative_slope=0.2)
        edge_score = jnp.exp(edge_score - jnp.max(edge_score))
        neigh_sums = jax.ops.segment_sum(edge_score, tgt_ind, num_segments=n_nodes)
        att_per_edge = edge_score / (neigh_sums[tgt_ind] + 1e-16)
        src_feat_weighted = proj_feat[src_ind] * att_per_edge[..., None]
        out_feat = jax.ops.segment_sum(src_feat_weighted, tgt_ind, num_segments=n_nodes)
        return out_feat.reshape(n_nodes, -1) + bias

    def _L3_gnn_ref(x, W1, b1, W2, b2, W3, b3, W4, b4, edge_index):
        import jax, jax.numpy as jnp
        import numpy as np
        N = 12500
        E = 200000
        D_IN, D_PROJ, D_HID = (128, 128, 64)

        def gcn_layer(x, W, b, src, dst, deg, inv_sqrt_deg):
            h = x @ W
            norm = inv_sqrt_deg[src] * inv_sqrt_deg[dst]
            agg = jax.ops.segment_sum(h[src] * norm[:, None], dst, num_segments=x.shape[0])
            agg = agg + h * (1.0 / deg)[:, None]
            return agg + b
        src, dst = (edge_index[0], edge_index[1])
        deg = jax.ops.segment_sum(jnp.ones(src.shape[0], x.dtype), dst, num_segments=x.shape[0]) + 1.0
        isd = jax.lax.rsqrt(deg)
        z = gcn_layer(x, W1, b1, src, dst, deg, isd)
        z = jax.nn.relu(z)
        z = gcn_layer(z, W2, b2, src, dst, deg, isd)
        z = gcn_layer(z, W3, b3, src, dst, deg, isd)
        z = jax.nn.relu(z)
        z = gcn_layer(z, W4, b4, src, dst, deg, isd)
        return z
    edge_index = jnp.stack([src, dst])
    x = _layernorm(x + _L0_gnn_ref(x, edge_index, L0_gnn_W, L0_gnn_att_src, L0_gnn_att_dst, L0_gnn_bias), axis=-1)
    x = _layernorm(x + _L1_gnn_ref(x, edge_index, edge_weight, edge_attr_50, L1_gnn_mlp_w0, L1_gnn_mlp_b0, L1_gnn_mlp_w2, L1_gnn_mlp_b2, L1_gnn_lin1_w, L1_gnn_lin2_w, L1_gnn_lin2_b, L1_gnn_lin_w, L1_gnn_lin_b), axis=-1)
    x = _layernorm(x + _L2_gnn_ref(x, edge_index, 200000, L2_gnn_W_proj, L2_gnn_a_src, L2_gnn_a_tgt, L2_gnn_bias), axis=-1)
    x = _layernorm(x + _L3_gnn_ref(x, L3_gnn_W1, L3_gnn_b1, L3_gnn_W2, L3_gnn_b2, L3_gnn_W3, L3_gnn_b3, L3_gnn_W4, L3_gnn_b4, edge_index), axis=-1)
    return x

_drawn_inputs = setup_inputs


def setup_inputs(seed=0):
    import zlib

    import numpy as np

    out = dict(_drawn_inputs(seed))
    spreads = {'L0_gnn_bias': (0.0, 0.1),
     'L1_gnn_mlp_b0': (0.0, 0.1),
     'L1_gnn_mlp_b2': (0.0, 0.1),
     'L1_gnn_lin2_b': (0.0, 0.1),
     'L1_gnn_lin_b': (0.0, 0.1),
     'L2_gnn_bias': (0.0, 0.1),
     'L3_gnn_b1': (0.0, 0.1),
     'L3_gnn_b2': (0.0, 0.1),
     'L3_gnn_b3': (0.0, 0.1),
     'L3_gnn_b4': (0.0, 0.1)}
    factors = {}
    for name, (base, spread) in spreads.items():
        noise = np.random.default_rng([zlib.crc32(name.encode()), seed]).standard_normal(out[name].shape)
        drawn = base * np.exp(spread * noise) if base else spread * noise
        out[name] = jnp.asarray(drawn.astype(out[name].dtype))
    for name, factor in factors.items():
        out[name] = (out[name] * factor).astype(out[name].dtype)
    return out
```

```python
from contextlib import ExitStack

import concourse.bass as bass
from concourse import mybir

ALU = mybir.AluOpType
ACT = mybir.ActivationFunctionType
AX = mybir.AxisListType.X
F32 = mybir.dt.float32
I32 = mybir.dt.int32
RMAX = bass.bass_isa.ReduceOp.max

N_NODES, N_EDGES, D, NF, HID, HEADS = 12500, 200000, 128, 50, 64, 4
C = D // HEADS
LANES = 128
ET = -(-N_EDGES // LANES)
REAL_NT = -(-N_NODES // LANES)
NT = 100
DUMMY = REAL_NT
GS = 8
NB = 4
STEP_COLS = -(-(ET + REAL_NT - 1) // LANES)
STEPS = STEP_COLS * LANES
GROUPS = STEPS // GS
AW = 136
BIG = 1e30
SAFE_RANGE = 60.0
LN_EPS = 1e-5
LOG_1E16 = 36.841361487904734
NM_GROUPS = NT // 2
PASSES = [("attend", 133, 132), ("filter", 128, 128), ("attend", 132, 132),
          ("plain", 128, 128), ("plain", 64, 64), ("plain", 64, 64), ("plain", 128, 128)]
PRODUCTS = [("x", 128, 136, False), ("x", 128, 128, False), ("acc", 128, 128, False), ("acc", 128, 128, False),
            ("x", 128, 136, False), ("x", 128, 128, True), ("acc", 128, 64, True), ("acc", 64, 128, False),
            ("acc", 128, 128, True)]
W_OF = [0, 2, 3, 4, 1, 5, 6, 7, 8]
BIASES = ["L0_gnn_bias", "L1_gnn_lin2_b", "L1_gnn_lin_b", "L2_gnn_bias", "L3_gnn_b1", "L3_gnn_b2", "L3_gnn_b3", "L3_gnn_b4"]

PI = 3.141592653589793
ROUND = 12582912.0
N_CONST = 16 + 9 + 2 + 8 + 4
BLOCKS = [(s, c) for s in range(3) for c in range(STEP_COLS)]
N_BLOCKS = -(-len(BLOCKS) // 4)


def build(nc, a, out, force_general=False, layers=4):
    with ExitStack() as ctx:
        def sb(name, shape, dt=F32):
            return ctx.enter_context(nc.sbuf_tensor(name, shape, dt))

        def sem(name):
            return ctx.enter_context(nc.semaphore(name))

        def dram(name, shape, dt=F32):
            return nc.dram_tensor(name, shape, dt).ap()

        tables = [dram(f"table{n}", [NT * LANES, w]) for n, w in enumerate([132, 128, 132, 128, 64, 64, 128])]
        plan_rows = dram("plan_rows", [2, ET])
        node_tile_dram = dram("node_tile_dram", [STEPS], I32)
        edge_tile_dram = dram("edge_tile_dram", [STEPS], I32)

        x = sb("x", [LANES, NT, D])
        acc = sb("acc", [LANES, NT, AW])
        rows = sb("rows", [LANES, NB, GS, AW])
        onehot = sb("onehot", [LANES, NB, GS, LANES])
        work = sb("work", [LANES, 4096])
        src_idx = sb("src_idx", [LANES, STEPS], I32)
        dst_loc = sb("dst_loc", [LANES, STEPS])
        edge_w = sb("edge_w", [LANES, STEPS])
        idx_buf = sb("idx_buf", [LANES, NB, GS], I32)
        node_tile = sb("node_tile", [1, STEPS], I32)
        edge_tile = sb("edge_tile", [1, STEPS], I32)
        adc = sb("adc", [LANES, NT, 2 * HEADS])
        weights = sb("weights", [LANES, 9, AW])
        mlp_w0 = sb("mlp_w0", [NF, LANES])
        mlp_w2 = sb("mlp_w2", [LANES, LANES])
        mlp_b0 = sb("mlp_b0", [LANES, 1])
        mlp_b2 = sb("mlp_b2", [1, LANES])
        bias = sb("bias", [LANES, 8, D])
        ones_row = sb("ones_row", [1, LANES])
        iota_i = sb("iota_i", [LANES, LANES], I32)
        iota_f = sb("iota_f", [LANES, LANES])
        part_i = sb("part_i", [LANES, STEP_COLS], I32)
        step_no = sb("step_no", [LANES, STEP_COLS])
        ident = sb("ident", [LANES, LANES])
        step_edge = sb("step_edge", [LANES, STEP_COLS])
        step_jump = sb("step_jump", [LANES, STEP_COLS])
        step_node = sb("step_node", [LANES, STEP_COLS])
        step_base = sb("step_base", [LANES, STEP_COLS])
        step_edge_i = sb("step_edge_i", [LANES, STEP_COLS], I32)
        step_node_i = sb("step_node_i", [LANES, STEP_COLS], I32)
        head_mix = sb("head_mix", [LANES, 2, 2 * HEADS])
        score = sb("score", [LANES, GS, HEADS])
        score2 = sb("score2", [LANES, GS, HEADS])
        score3 = sb("score3", [LANES, GS, HEADS])
        best = sb("best", [LANES, GS, HEADS])
        extremes = sb("extremes", [LANES, 2 * HEADS])
        extremes_all = sb("extremes_all", [LANES, 2 * HEADS])
        best_all = sb("best_all", [LANES, 2])
        spread = sb("spread", [LANES, HEADS])
        flag_f = sb("flag_f", [LANES, 1])
        flag = sb("flag", [LANES, 1], I32)
        stat = sb("stat", [LANES, NT])
        stat2 = sb("stat2", [LANES, NT])
        degree = sb("degree", [LANES, NT])
        inv_root = sb("inv_root", [LANES, NT])
        node4 = sb("node4", [LANES, NT, HEADS])
        node4b = sb("node4b", [LANES, NT, HEADS])
        half_eps = sb("half_eps", [LANES, 2])

        ps_t = ctx.enter_context(nc.psum_tensor("ps_t", [LANES, 2, 512], F32))
        ps_a = ctx.enter_context(nc.psum_tensor("ps_a", [LANES, 2, 512], F32))
        ps_m = ctx.enter_context(nc.psum_tensor("ps_m", [LANES, 4, 512], F32))

        zeroed = sem("zeroed")
        plan_rows_made = sem("plan_rows_made")
        consts_in = sem("consts_in")
        x_in = sem("x_in")
        ends_in = sem("ends_in")
        plan_out = sem("plan_out")
        plan_in = sem("plan_in")
        iotas = sem("iotas")
        made = sem("made")
        plan_ready = sem("plan_ready")
        tiles_out = sem("tiles_out")
        tiles_in = sem("tiles_in")
        lists_in = sem("lists_in")
        lists_turned = sem("lists_turned")
        lists_kept = sem("lists_kept")
        mixed = sem("mixed")
        shift_made = sem("shift_made")
        self_scored = sem("self_scored")
        self_exp = sem("self_exp")
        tanh_asked = sem("tanh_asked")
        tanh_done = sem("tanh_done")
        centred = sem("centred")
        squared = sem("squared")
        var_made = sem("var_made")
        root_made = sem("root_made")
        best_made = sem("best_made")
        best_reduced = sem("best_reduced")
        guard_asked = sem("guard_asked")
        guard_exp = sem("guard_exp")
        phase_made = sem("phase_made")
        sine_made = sem("sine_made")
        degree_made = sem("degree_made")
        degree_root = sem("degree_root")
        ssp_asked = sem("ssp_asked")
        ssp_log = sem("ssp_log")
        ssp_added = sem("ssp_added")
        out_ready = sem("out_ready")
        list_floats = sem("list_floats")
        mix_kept = sem("mix_kept")
        consts_made = sem("consts_made")
        nm_from = sem("nm_from")
        nm_staged = sem("nm_staged")
        nm_turned = sem("nm_turned")
        nm_copied = sem("nm_copied")
        nm_done = sem("nm_done")
        nm_kept = sem("nm_kept")
        table_made = sem("table_made")
        table_out = sem("table_out")
        extremes_made = sem("extremes_made")
        extremes_reduced = sem("extremes_reduced")
        flag_made = sem("flag_made")
        gen_idx = [sem(f"gen_idx{n}") for n in range(2)]
        gen_in = [sem(f"gen_in{n}") for n in range(2)]
        gen_made = [sem(f"gen_made{n}") for n in range(2)]
        gen_chain = [sem(f"gen_chain{n}") for n in range(2)]
        gen_turned = [sem(f"gen_turned{n}") for n in range(2)]
        gen_max = [sem(f"gen_max{n}") for n in range(2)]
        idx_copied = sem("idx_copied")
        gathered = [sem(f"gathered{b}") for b in range(NB)]
        onehot_ready = sem("onehot_ready")
        turned = sem("turned")
        turned_kept = sem("turned_kept")
        dst_ready = sem("dst_ready")
        score_chain = sem("score_chain")
        scored = sem("scored")
        exp_ready = sem("exp_ready")
        msg_ready = sem("msg_ready")
        part_ready = sem("part_ready")
        part_added = sem("part_added")
        pool_turn = sem("pool_turn")
        edge_in = [sem(f"edge_in{b}") for b in range(2)]
        layer1_ready = sem("layer1_ready")
        act_chain = sem("act_chain")
        ssp_ready = sem("ssp_ready")
        layer2_ready = sem("layer2_ready")
        out_done = sem("out_done")

        dst_rows = a["dst"].rearrange("(t e) -> t e", e=LANES)
        src_rows = a["src"].rearrange("(t e) -> t e", e=LANES)
        w_rows = a["edge_weight"].rearrange("(t e) -> t e", e=LANES)

        xt = [work[:, 256 * b:256 * b + 256] for b in range(2)]
        stage = [work[:, 512 + 256 * b:768 + 256 * b] for b in range(2)]
        onehot_t = [work[:, 1024 * b:1024 * b + 1024] for b in range(2)]
        ssp_a = [work[:, 512 * q:512 * q + 512] for q in range(2)]
        ssp_r = [work[:, 1024 + 512 * q:1536 + 512 * q] for q in range(2)]
        edge_x = [work[0:NF, 2048 + 1024 * b:3072 + 1024 * b] for b in range(2)]
        flat = onehot[:, :, :, :].rearrange("p b k n -> p (b k n)")
        start_b, jump_b, cmp_b = flat[:, 0:ET], flat[:, ET:2 * ET], work[:, 0:ET]
        rows_flat = rows[:, :, :, :].rearrange("p b k n -> p (b k n)")
        dst_list, src_list, w_list = rows_flat[:, 0:STEPS], rows_flat[:, STEPS:2 * STEPS], flat[:, 0:STEPS]
        dst_list_f, src_list_f = flat[:, STEPS:2 * STEPS], work[:, 0:STEPS]
        acc_flat = acc[:, :, :].rearrange("p t w -> p (t w)")
        first_i, last_i, first_f, last_f, span_row, start_row, jump_row, ones_e = [
            acc_flat[0:1, n * ET:(n + 1) * ET] for n in range(8)]
        weights_t = [rows_flat[:, 2 * STEPS + LANES * n:2 * STEPS + LANES * (n + 1)] for n in range(2)]

        heads = lambda ap: ap.rearrange("p t (h c) -> p t h c", c=C)
        spread_heads = lambda ap, n: ap.unsqueeze(3).to_broadcast([LANES, n, HEADS, C])
        over_nodes = lambda ap, w: ap.unsqueeze(2).to_broadcast([LANES, NT, w])
        over_tiles = lambda n, w: bias[:, n, 0:w].unsqueeze(1).to_broadcast([LANES, NT, w])

        ATTEND = {0: 0, 2: 1}
        MSG = {0: 0, 1: 1, 2: 2}
        ssp_tmp = [f[:, 0:25 * D].rearrange("p (t f) -> p t f", f=D) for f in (rows_flat, flat)]

        block = ctx.enter_context(nc.Block())

        class Turn:

            def __init__(self, j, i=None, u=None):
                self.j, self.i, self.u = j, i, u

            def has(self, d):
                return self.i is not None or 0 <= self.j + d < GROUPS

            def g(self, d):
                return self.j + d

            def b(self, d, n=NB):
                return ((self.j if self.i is None else self.u) + d) % n

            def before(self, d, n=NB):
                return (self.j + d) // n if self.i is None else self.i * (NB // n) + (self.u + d) // n

        def over_groups(eng, body):
            body(Turn(-1))
            body(Turn(0))
            turns = (GROUPS - NB) // NB
            with eng.Fori(0, turns) as i:
                for u in range(1, 1 + NB):
                    body(Turn(i * NB + u, i, u))
            for j in range(1 + turns * NB, GROUPS + 1):
                body(Turn(j))

        def registers(engine, ap, top):
            return nc.values_load_multi_w_load_instructions(
                ap, engines=[engine], min_val=0, max_val=top,
                skip_runtime_bounds_check_because="the plan keeps it below that")[1]

        @block.sync
        def _(sp):
            with nc.allow_non_contiguous_dma("one element of each edge tile"):
                sp.dma_start(first_i.bitcast(I32), dst_rows[:, 0:1].rearrange("t e -> e t")).then_inc(ends_in, 16)
                sp.dma_start(last_i.bitcast(I32), dst_rows[:, LANES - 1:LANES].rearrange("t e -> e t")).then_inc(ends_in, 16)
            sp.dma_start(x[:, :, :], a["x"].rearrange("(t p) f -> p t f", p=LANES)).then_inc(x_in, 16)
            sp.wait_ge(zeroed, 1)
            n_const = 0

            def const(dst, src):
                nonlocal n_const
                n_const += 1
                sp.dma_start(dst, src).then_inc(consts_in, 16)

            for n, names in enumerate((("L0_gnn_att_src", "L0_gnn_att_dst"), ("L2_gnn_a_src", "L2_gnn_a_tgt"))):
                for j, name in enumerate(names):
                    for h in range(HEADS):
                        const(head_mix[C * h:C * h + C, n, HEADS * j + h:HEADS * j + h + 1],
                              a[name][h * C:(h + 1) * C].rearrange("(c o) -> c o", o=1))
            for col, name in enumerate(("L0_gnn_W", "L2_gnn_W_proj", "L1_lin1_wT", "L1_lin2_wT", "L1_lin_wT",
                                        "L3_gnn_W1", "L3_gnn_W2", "L3_gnn_W3", "L3_gnn_W4")):
                k, m = a[name].shape
                const(weights[0:k, col, 0:m], a[name])
            for n, name in enumerate(("L0_WT", "L2_WT")):
                const(weights_t[n], a[name])
            for n, name in enumerate(BIASES):
                w = a[name].shape[0]
                const(bias[:, n, 0:w], a[name].rearrange("(o f) -> o f", o=1).to_broadcast([LANES, w]))
            const(mlp_w0[:, :], a["L1_mlp_w0T"])
            const(mlp_w2[:, :], a["L1_mlp_w2T"])
            const(mlp_b0[:, :], a["L1_gnn_mlp_b0"].rearrange("(f o) -> f o", o=1))
            const(mlp_b2[:, :], a["L1_gnn_mlp_b2"].rearrange("(o f) -> o f", o=1))
            assert n_const == N_CONST, n_const
            sp.wait_ge(plan_rows_made, 1)
            sp.dma_start(plan_rows[0:1, :], start_row).then_inc(plan_out, 16)
            sp.dma_start(plan_rows[1:2, :], jump_row).then_inc(plan_out, 16)
            sp.wait_ge(plan_out, 32)
            sp.dma_start(start_b, plan_rows[0:1, :].to_broadcast([LANES, ET])).then_inc(plan_in, 16)
            sp.dma_start(jump_b, plan_rows[1:2, :].to_broadcast([LANES, ET])).then_inc(plan_in, 16)
            sp.wait_ge(plan_ready, 1)
            with nc.allow_non_contiguous_dma("13 columns"):
                sp.dma_start(node_tile_dram.rearrange("(c p) -> p c", p=LANES), step_node_i[:, :]).then_inc(tiles_out, 16)
                sp.dma_start(edge_tile_dram.rearrange("(c p) -> p c", p=LANES), step_edge_i[:, :]).then_inc(tiles_out, 16)
            sp.wait_ge(tiles_out, 32)
            sp.dma_start(node_tile[:, :], node_tile_dram.rearrange("(o s) -> o s", o=1)).then_inc(tiles_in, 16)
            sp.dma_start(edge_tile[:, :], edge_tile_dram.rearrange("(o s) -> o s", o=1)).then_inc(tiles_in, 16)

            def table(n):
                sp.wait_ge(table_made, n + 1)
                w = tables[n].shape[1]
                sp.dma_start(tables[n].rearrange("(t p) w -> p t w", p=LANES), acc[:, :, 0:w]).then_inc(table_out, 16)

            def edge_features(g, b):
                sp.wait_ge(layer1_ready, g * 2 + 2)
                tile = registers(mybir.EngineType.SP, edge_tile[0:1, bass.ds(g * GS, GS)], ET - 1)
                for k in range(GS):
                    sp.dma_start(edge_x[b][:, LANES * k:LANES * k + LANES],
                                 a["edge_attr_t"][bass.ds(tile[k], 1), :, :].rearrange("o f e -> (o f) e")
                                 ).then_inc(edge_in[b], 16)

            sp.wait_ge(tiles_in, 32)
            table(0)
            if layers > 1:
                table(1)
                with sp.Fori(0, GROUPS // 2) as i:
                    for b in range(2):
                        edge_features(i * 2 + b, b)
            for n in range(2, (0, 1, 2, 3, 7)[layers]):
                table(n)
            sp.wait_ge(out_ready, 1)
            full = N_NODES // LANES
            sp.dma_start(out[0:full * LANES, :].rearrange("(t p) f -> p t f", p=LANES), x[:, 0:full, :]).then_inc(out_done, 16)
            sp.dma_start(out[full * LANES:N_NODES, :], x[0:N_NODES - full * LANES, full, :]).then_inc(out_done, 16)
            sp.wait_ge(out_done, 32)

        @block.gpsimd
        def _(pool):
            pool.memset(head_mix[:, :, :], 0.0)
            pool.memset(weights[:, :, :], 0.0)
            pool.memset(bias[:, :, :], 0.0).then_inc(zeroed, 1)
            pool.iota(iota_i[:, :], pattern=[[1, LANES]], base=0, channel_multiplier=0)
            pool.iota(part_i[:, :], pattern=[[LANES, STEP_COLS]], base=0, channel_multiplier=1).then_inc(iotas, 1)
            pool.wait_ge(plan_ready, 1)
            pool.wait_ge(mix_kept, 1)
            for c in range(STEP_COLS):
                for dst, src in ((dst_list.bitcast(I32), dst_rows), (src_list.bitcast(I32), src_rows), (w_list, w_rows)):
                    pool.indirect_dma_start(dst[:, LANES * c:LANES * (c + 1)], None, src,
                                            bass.IndirectOffsetOnAxis(step_edge_i[:, c:c + 1], 0)).then_inc(lists_in, 16)

            def general_shift(n):
                flagged = pool.value_load(flag[0:1, 0:1], min_val=0, max_val=1)
                with pool.If(flagged == 1):
                    with pool.Fori(0, STEPS) as s:
                        pool.wait_ge(gen_idx[n], s + 1)
                        pool.sem_inc(pool_turn, 1)
                        pool.indirect_dma_start(rows[:, 0, 0, 0:132], None, tables[2 * n],
                                                bass.IndirectOffsetOnAxis(idx_buf[:, 0, 0:1], 0)).then_inc(gen_in[n], 16)
                with pool.Else():
                    pool.nop()
                pool.nop()

            def gathers(n):
                w = tables[n].shape[1]
                pool.wait_ge(table_out, 16 * (n + 1))
                if n in ATTEND:
                    k = ATTEND[n]
                    pool.wait_ge(extremes_made, k + 1)
                    pool.partition_all_reduce(extremes_all[:, :], extremes[:, :], LANES, RMAX).then_inc(extremes_reduced, 1)
                    pool.wait_ge(flag_made, k + 1)
                    general_shift(k)
                with pool.Fori(0, GROUPS // NB) as i:
                    for b in range(NB):
                        pool.wait_ge(idx_copied, n * GROUPS + i * NB + b + 1)
                        pool.sem_inc(pool_turn, 1)
                        for k in range(GS):
                            pool.indirect_dma_start(rows[:, b, k, 0:w], None, tables[n],
                                                    bass.IndirectOffsetOnAxis(idx_buf[:, b, k:k + 1], 0)
                                                    ).then_inc(gathered[b], 16)

            for n in range((0, 1, 2, 3, 7)[layers]):
                gathers(n)
                if n == 2:
                    pool.wait_ge(best_made, 1)
                    pool.partition_all_reduce(best_all[:, 1:2], best_all[:, 0:1], LANES, RMAX).then_inc(best_reduced, 1)

        @block.tensor
        def _(pe):
            pe.sem_inc(part_ready, NB * GS)
            pe.sem_inc(dst_ready, 2)
            pe.sem_inc(layer1_ready, 4)
            pe.sem_inc(layer2_ready, 2)
            pe.sem_inc(nm_done, 2)
            pe.sem_inc(nm_turned, 2)
            pe.wait_ge(consts_in, 16 * N_CONST)
            for n in range(2):
                mm = pe.matmul(ps_a[:, n, 0:2 * HEADS], weights_t[n], head_mix[:, n, :], start=True, stop=True)
            mm.then_inc(mixed, 1)
            pe.wait_ge(lists_in, 16 * 3 * STEP_COLS)
            pe.wait_ge(list_floats, 1)
            for m in range(N_BLOCKS):
                if m >= 2:
                    pe.wait_ge(lists_kept, m - 1)
                for k, (src, c) in enumerate(BLOCKS[4 * m:4 * m + 4]):
                    mm = pe.transpose(ps_t[:, m % 2, LANES * k:LANES * k + LANES],
                                      (dst_list_f, src_list_f, w_list)[src][:, LANES * c:LANES * (c + 1)], ident[:, :])
                mm.then_inc(lists_turned, 1)

            def product(m):
                _, k, w, _ = PRODUCTS[m]
                base = m * NM_GROUPS

                def turn(v, b):
                    pe.wait_ge(nm_copied, base + v + 1)
                    pe.wait_ge(nm_staged, base + v + 1)
                    for t in range(2):
                        mm = pe.transpose(ps_t[:, b, LANES * t:LANES * t + LANES],
                                          stage[b][:, LANES * t:LANES * t + LANES], ident[:, :])
                    mm.then_inc(nm_turned, 1)

                def multiply(v, b):
                    pe.wait_ge(nm_copied, base + v + 3)
                    pe.wait_ge(nm_kept, base + v + 1)
                    for t in range(2):
                        mm = pe.matmul(ps_a[:, b, w * t:w * t + w], xt[b][0:k, LANES * t:LANES * t + LANES],
                                       weights[0:k, W_OF[m], 0:w], start=True, stop=True)
                    mm.then_inc(nm_done, 1)

                turn(0, 0)
                with pe.Fori(0, NM_GROUPS // 2 - 1) as i:
                    for u in range(2):
                        turn(i * 2 + u + 1, (u + 1) % 2)
                        multiply(i * 2 + u, u)
                turn(NM_GROUPS - 1, 1)
                multiply(NM_GROUPS - 2, 0)
                multiply(NM_GROUPS - 1, 1)

            def general_shift(n):
                pe.wait_ge(flag_made, n + 1)
                flagged = pe.value_load(flag[0:1, 0:1], min_val=0, max_val=1)
                with pe.If(flagged == 1):
                    with pe.Fori(0, STEPS) as s:
                        pe.wait_ge(gen_made[n], s + 1)
                        for h in range(HEADS):
                            mm = pe.transpose(ps_t[:, 0, LANES * h:LANES * h + LANES], onehot[:, 0, 2 + h, :], ident[:, :])
                        mm.then_inc(gen_turned[n], 1)
                with pe.Else():
                    pe.nop()
                pe.nop()

            def sums(n):
                kind, w, _ = PASSES[n]

                def main(T):
                    g, b = T.g(-1), T.b(-1)
                    if kind == "plain":
                        pe.wait_ge(onehot_ready, n * GROUPS + g + 1)
                        pe.wait_ge(gathered[b], 16 * GS * (n * (GROUPS // NB) + T.before(-1) + 1))
                    else:
                        pe.wait_ge(msg_ready, MSG[n] * GROUPS + g + 1)
                    for k in range(GS):
                        pe.wait_ge(part_added, n * STEPS + g * GS + k + 1)
                        mm = pe.matmul(ps_m[:, k % 4, 0:w], onehot[:, b, k, :], rows[:, b, k, 0:w], start=True, stop=True)
                        mm.then_inc(part_ready, 1)

                def attend(T):
                    if T.has(1):
                        g, b, b2 = T.g(1), T.b(1), T.b(1, 2)
                        pe.wait_ge(onehot_ready, n * GROUPS + g + 1)
                        for q in range(2):
                            pe.wait_ge(turned_kept, ATTEND[n] * 2 * GROUPS + g * 2 + q + 1)
                            for k in range(4):
                                mm = pe.transpose(ps_t[:, q, LANES * k:LANES * k + LANES], onehot[:, b, 4 * q + k, :], ident[:, :])
                            mm.then_inc(turned, 1)
                    if T.has(-1):
                        main(T)
                    if T.has(1):
                        tile = registers(mybir.EngineType.PE, node_tile[0:1, bass.ds(g * GS, GS)], NT - 1)
                        pe.wait_ge(turned_kept, ATTEND[n] * 2 * GROUPS + g * 2 + 4)
                        pe.wait_ge(scored, ATTEND[n] * GROUPS + g + 1)
                        for k in range(GS):
                            mm = pe.matmul(ps_a[:, b2, 2 * HEADS * k:2 * HEADS * (k + 1)],
                                           onehot_t[b2][:, LANES * k:LANES * k + LANES],
                                           adc[:, bass.ds(tile[k], 1), :].rearrange("p o f -> p (o f)"), start=True, stop=True)
                        mm.then_inc(dst_ready, 1)

                def edge_filter(T):
                    if T.has(0):
                        g = T.g(0)
                        pe.wait_ge(msg_ready, MSG[n] * GROUPS + g)
                        for q in range(2):
                            pe.wait_ge(ssp_ready, g * 2 + q + 1)
                            for k in range(4):
                                pe.matmul(ps_a[:, q, LANES * k:LANES * k + LANES], ones_row[:, :], mlp_b2[:, :], start=True, stop=False)
                                mm = pe.matmul(ps_a[:, q, LANES * k:LANES * k + LANES],
                                               ssp_r[q][:, LANES * k:LANES * k + LANES], mlp_w2[:, :],
                                               start=False, stop=True)
                            mm.then_inc(layer2_ready, 1)
                    if T.has(1):
                        g, b2 = T.g(1), T.b(1, 2)
                        pe.wait_ge(edge_in[b2], 16 * GS * (T.before(1, 2) + 1))
                        for q in range(2):
                            pe.wait_ge(act_chain, g * 8 + 2 * (q + 1))
                            mm = pe.matmul(ps_t[:, q, :], mlp_w0[:, :], edge_x[b2][:, 512 * q:512 * q + 512], start=True, stop=True)
                            mm.then_inc(layer1_ready, 1)
                    if T.has(-1):
                        main(T)

                def plain(T):
                    if T.has(-1):
                        main(T)

                over_groups(pe, {"attend": attend, "filter": edge_filter, "plain": plain}[kind])

            pe.wait_ge(mix_kept, 1)
            product(0)
            general_shift(0)
            sums(0)
            if layers > 1:
                product(1)
                sums(1)
                product(2)
                product(3)
            if layers > 2:
                product(4)
                general_shift(1)
                sums(2)
            if layers > 3:
                product(5)
                sums(3)
                product(6)
                sums(4)
                sums(5)
                product(7)
                product(8)
                sums(6)

        @block.scalar
        def _(act):
            act.sem_inc(turned_kept, 2)
            act.sem_inc(nm_copied, 2)
            act.sem_inc(act_chain, 8)
            act.wait_ge(phase_made, 1)
            act.activation(edge_w[:, :], edge_w[:, :], ACT.Sin, scale=PI).then_inc(sine_made, 1)

            def product(m):
                src = PRODUCTS[m][0]
                base = m * NM_GROUPS
                rows_of = x if src == "x" else acc

                def put(v, b):
                    act.wait_ge(nm_turned, base + v + 1)
                    act.copy(stage[b].rearrange("p (t f) -> p t f", t=2), rows_of[:, bass.ds(v * 2, 2), 0:D]).then_inc(nm_staged, 1)

                def copy(v, b):
                    act.wait_ge(nm_turned, base + v + 3)
                    act.wait_ge(nm_done, base + v + 1)
                    act.copy(xt[b], ps_t[:, b, 0:2 * LANES]).then_inc(nm_copied, 1)

                act.wait_ge(nm_from, m + 1)
                put(0, 0)
                with act.Fori(0, NM_GROUPS // 2 - 1) as i:
                    for u in range(2):
                        put(i * 2 + u + 1, (u + 1) % 2)
                        copy(i * 2 + u, u)
                put(NM_GROUPS - 1, 1)
                copy(NM_GROUPS - 2, 0)
                copy(NM_GROUPS - 1, 1)

            def indices(n, g, b):
                act.wait_ge(part_ready, n * STEPS + g * GS + GS)
                act.copy(idx_buf[:, b, :], src_idx[:, bass.ds(g * GS, GS)]).then_inc(idx_copied, 1)

            def ahead(n, T):
                if T.i is None and T.j == -1:
                    for g in range(3):
                        indices(n, g, g)
                elif T.has(3):
                    indices(n, T.g(3), T.b(3))

            def sums(n):
                def attend(T):
                    if T.has(1):
                        g, b2 = T.g(1), T.b(1, 2)
                        act.wait_ge(dst_ready, ATTEND[n] * GROUPS + g + 1)
                        for q in range(2):
                            act.wait_ge(turned, ATTEND[n] * 2 * GROUPS + g * 2 + q + 1)
                            act.copy(onehot_t[b2][:, 512 * q:512 * q + 512], ps_t[:, q, :]).then_inc(turned_kept, 1)
                    if T.has(0):
                        act.wait_ge(scored, ATTEND[n] * GROUPS + T.g(0) + 3)
                        act.activation(rows[:, T.b(0), :, D:D + HEADS], score[:, :, :], ACT.Exp).then_inc(exp_ready, 1)
                    ahead(n, T)

                def edge_filter(T):
                    ahead(n, T)
                    if T.has(1):
                        g = T.g(1)
                        step = g * 8 + 8
                        for q in range(2):
                            act.wait_ge(layer1_ready, g * 2 + q + 5)
                            act.wait_ge(layer2_ready, g * 2 + q + 1)
                            act.activation(ssp_r[q], ps_t[:, q, :], ACT.Relu, bias=mlp_b0[:, 0:1]).then_inc(act_chain, 1)
                            act.activation(ssp_a[q], ps_t[:, q, :], ACT.Abs, bias=mlp_b0[:, 0:1]).then_inc(act_chain, 1)
                        for q in range(2):
                            act.wait_ge(act_chain, step + 2 * (q + 1))
                            act.activation(ssp_a[q], ssp_a[q], ACT.Exp, scale=-1.0).then_inc(act_chain, 1)
                        for q in range(2):
                            act.wait_ge(act_chain, step + 4 + q + 1)
                            act.activation(ssp_a[q], ssp_a[q], ACT.Ln, scale=0.5, bias=half_eps[:, 0:1]).then_inc(act_chain, 1)

                def plain(T):
                    ahead(n, T)

                over_groups(act, {"attend": attend, "filter": edge_filter, "plain": plain}[PASSES[n][0]])

            def norm(l):
                act.wait_ge(centred, l + 1)
                act.activation(acc[:, :, 0:D], x[:, :, :], ACT.Square).then_inc(squared, 1)
                act.wait_ge(var_made, l + 1)
                act.activation(stat[:, :], stat[:, :], ACT.Sqrt).then_inc(root_made, 1)

            product(0)
            act.wait_ge(self_scored, 1)
            act.activation(acc[:, :, D:D + HEADS], node4[:, :, :], ACT.Exp).then_inc(self_exp, 1)
            sums(0)
            act.wait_ge(tanh_asked, 1)
            act.activation(acc[:, :, 0:D], acc[:, :, 0:D], ACT.Tanh).then_inc(tanh_done, 1)
            norm(0)
            if layers > 1:
                product(1)
                sums(1)
                product(2)
                act.wait_ge(ssp_asked, 1)
                for q in range(4):
                    if q >= 2:
                        act.wait_ge(ssp_added, q - 1)
                    part, tmp = acc[:, 25 * q:25 * q + 25, 0:D], ssp_tmp[q % 2]
                    act.activation(tmp, part, ACT.Abs).then_inc(ssp_log, 1)
                    act.wait_ge(ssp_log, 3 * q + 1)
                    act.activation(tmp, tmp, ACT.Exp, scale=-1.0).then_inc(ssp_log, 1)
                    act.wait_ge(ssp_log, 3 * q + 2)
                    act.activation(tmp, tmp, ACT.Ln, scale=0.5, bias=half_eps[:, 0:1]).then_inc(ssp_log, 1)
                product(3)
                norm(1)
            if layers > 2:
                product(4)
                sums(2)
                act.wait_ge(guard_asked, 1)
                act.activation(node4b[:, :, :], node4[:, :, :], ACT.Exp).then_inc(guard_exp, 1)
                norm(2)
            if layers > 3:
                act.wait_ge(degree_made, 1)
                act.activation(inv_root[:, :], degree[:, :], ACT.Sqrt).then_inc(degree_root, 1)
                product(5)
                sums(3)
                product(6)
                sums(4)
                sums(5)
                product(7)
                product(8)
                sums(6)
                norm(3)

        @block.vector
        def _(dve):
            counts = {}

            def link(ins, s=made):
                counts[s.name] = counts.get(s.name, 0) + 1
                ins.then_inc(s, 1)
                dve.wait_ge(s, counts[s.name])

            dve.sem_inc(part_added, 4)
            dve.sem_inc(nm_kept, 2)
            dve.sem_inc(scored, 2)
            dve.memset(ones_row[:, :], 1.0)
            dve.memset(half_eps[:, :], 0.5)
            dve.memset(ones_e, 1.0)
            dve.wait_ge(iotas, 1)
            dve.tensor_copy(iota_f[:, :], iota_i[:, :])
            link(dve.tensor_copy(step_no[:, :], part_i[:, :]))
            link(dve.tensor_scalar(ident[:, :], iota_f[:, :], step_no[:, 0:1], None, ALU.is_equal), consts_made)
            dve.wait_ge(ends_in, 32)
            for i_row, f_row in ((first_i, first_f), (last_i, last_f)):
                link(dve.tensor_scalar(i_row.bitcast(I32), i_row.bitcast(I32), 7, None, ALU.logical_shift_right))
                link(dve.tensor_copy(f_row, i_row.bitcast(I32)))
            link(dve.tensor_tensor(span_row, last_f, first_f, ALU.subtract))
            link(dve.tensor_tensor_scan(start_row, span_row, ones_e, 0.0, ALU.add, ALU.add))
            link(dve.scalar_tensor_tensor(start_row, start_row, -1.0, span_row, ALU.add, ALU.subtract))
            dve.tensor_copy(jump_row[:, 0:1], first_f[:, 0:1])
            link(dve.tensor_tensor(jump_row[:, 1:ET], first_f[:, 1:ET], last_f[:, 0:ET - 1], ALU.subtract), plan_rows_made)
            dve.wait_ge(mixed, 1)
            for n in range(2):
                ins = dve.tensor_copy(weights[:, n, D:AW], ps_a[:, n, 0:2 * HEADS])
            link(ins, mix_kept)
            dve.wait_ge(plan_in, 32)
            for c in range(STEP_COLS):
                link(dve.scalar_tensor_tensor(cmp_b, start_b, step_no[:, c:c + 1], jump_b, ALU.is_le, ALU.mult,
                                              accum_out=step_jump[:, c:c + 1]))
                link(dve.tensor_scalar(cmp_b, start_b, step_no[:, c:c + 1], 0.0, ALU.is_le, ALU.add,
                                       accum_out=step_edge[:, c:c + 1]))
            link(dve.tensor_scalar(step_edge[:, :], step_edge[:, :], -1.0, None, ALU.add))
            link(dve.tensor_tensor(step_node[:, :], step_no[:, :], step_edge[:, :], ALU.subtract))
            link(dve.tensor_tensor(step_node[:, :], step_node[:, :], step_jump[:, :], ALU.add))
            link(dve.tensor_scalar(step_node[:, :], step_node[:, :], float(DUMMY), None, ALU.min))
            dve.tensor_scalar(step_base[:, :], step_node[:, :], float(LANES), None, ALU.mult)
            dve.tensor_copy(step_node_i[:, :], step_node[:, :])
            link(dve.tensor_copy(step_edge_i[:, :], step_edge[:, :]), plan_ready)
            dve.wait_ge(lists_in, 16 * 3 * STEP_COLS)
            for c in range(STEP_COLS):
                cols = slice(LANES * c, LANES * (c + 1))
                dve.tensor_scalar(dst_list_f[:, cols], dst_list[:, cols].bitcast(I32), step_base[:, c:c + 1], None, ALU.subtract)
            link(dve.tensor_copy(src_list_f, src_list.bitcast(I32)), list_floats)
            for m in range(N_BLOCKS):
                dve.wait_ge(lists_turned, m + 1)
                blocks = BLOCKS[4 * m:4 * m + 4]
                for k, (src, c) in enumerate(blocks):
                    ins = dve.tensor_copy((dst_loc, src_idx, edge_w)[src][:, LANES * c:LANES * (c + 1)],
                                          ps_t[:, m % 2, LANES * k:LANES * k + LANES])
                link(ins, lists_kept)
            link(dve.tensor_scalar(edge_w[:, :], edge_w[:, :], 0.05, None, ALU.mult))
            link(dve.tensor_scalar(work[:, 0:STEPS], edge_w[:, :], ROUND, None, ALU.add))
            link(dve.tensor_scalar(work[:, 0:STEPS], work[:, 0:STEPS], ROUND, None, ALU.subtract))
            link(dve.tensor_tensor(edge_w[:, :], edge_w[:, :], work[:, 0:STEPS], ALU.subtract), phase_made)
            dve.wait_ge(sine_made, 1)
            link(dve.tensor_tensor(edge_w[:, :], edge_w[:, :], edge_w[:, :], ALU.mult))
            link(dve.tensor_scalar(edge_w[:, :], edge_w[:, :], -1.0, 1.0, ALU.mult, ALU.add))
            link(dve.memset(rows[:, :, :, D + HEADS:D + HEADS + 1], 1.0))

            feats = acc[:, :, 0:D]

            def product(m):
                _, _, w, scaled = PRODUCTS[m]
                base = m * NM_GROUPS
                with dve.Fori(0, NM_GROUPS // 2) as i:
                    for u in range(2):
                        dve.wait_ge(nm_done, base + i * 2 + u + 3)
                        v = i * 2 + u
                        src = ps_a[:, u, 0:2 * w].rearrange("p (t w) -> p t w", t=2)
                        dst = acc[:, bass.ds(v * 2, 2), 0:w]
                        if scaled:
                            ins = dve.tensor_tensor(dst, src, inv_root[:, bass.ds(v * 2, 2)].unsqueeze(2).to_broadcast([LANES, 2, w]), ALU.mult)
                        else:
                            ins = dve.tensor_copy(dst, src)
                        ins.then_inc(nm_kept, 1)
                dve.wait_ge(nm_kept, base + NM_GROUPS + 2)

            def table_ready(n):
                dve.drain().then_inc(table_made, 1)
                dve.wait_ge(table_out, 16 * (n + 1))

            def general_shift(n):
                with dve.Fori(0, STEPS) as s:
                    at = s * 8
                    dve.tensor_copy(idx_buf[:, 0, 0:1], src_idx[:, bass.ds(s, 1)]).then_inc(gen_idx[n], 1)
                    one, off = onehot[:, 0, 0, :], onehot[:, 0, 1, :]
                    dve.tensor_scalar(one, iota_f[:, :], dst_loc[:, bass.ds(s, 1)], None, ALU.is_equal).then_inc(gen_chain[n], 1)
                    dve.wait_ge(gen_chain[n], at + 1)
                    dve.tensor_scalar(off, one, BIG, -BIG, ALU.mult, ALU.add).then_inc(gen_chain[n], 1)
                    dve.wait_ge(gen_chain[n], at + 2)
                    dve.wait_ge(gen_in[n], s * 16 + 16)
                    for h in range(HEADS):
                        dve.scalar_tensor_tensor(onehot[:, 0, 2 + h, :], one, rows[:, 0, 0, D + h:D + h + 1], off,
                                                 ALU.mult, ALU.add).then_inc(gen_chain[n], 1)
                    dve.wait_ge(gen_chain[n], at + 6)
                    dve.sem_inc(gen_made[n], 1)
                    tile = registers(mybir.EngineType.DVE, node_tile[0:1, bass.ds(s, 1)], NT - 1)[0]
                    dve.wait_ge(gen_turned[n], s + 1)
                    dve.tensor_reduce(score[:, 0, :], ps_t[:, 0, :].rearrange("p (h e) -> p h e", h=HEADS), AX, ALU.max).then_inc(gen_chain[n], 1)
                    dve.wait_ge(gen_chain[n], at + 7)
                    shift = adc[:, bass.ds(tile, 1), HEADS:2 * HEADS].rearrange("p o h -> p (o h)")
                    dve.tensor_tensor(shift, shift, score[:, 0, :], ALU.max).then_inc(gen_chain[n], 1)
                    dve.wait_ge(gen_chain[n], at + 8)

            def shifts(n):
                k = ATTEND[n]
                src_score = acc[:, :, D:D + HEADS]
                dve.tensor_copy(adc[:, :, 0:HEADS], acc[:, :, D + HEADS:AW])
                dve.tensor_reduce(extremes[:, 0:HEADS], src_score.rearrange("p t h -> p h t"), AX, ALU.max)
                link(dve.tensor_reduce(extremes[:, HEADS:2 * HEADS], src_score.rearrange("p t h -> p h t"), AX, ALU.min))
                link(dve.tensor_scalar(extremes[:, HEADS:2 * HEADS], extremes[:, HEADS:2 * HEADS], -1.0, None, ALU.mult), extremes_made)
                dve.wait_ge(extremes_reduced, k + 1)
                link(dve.tensor_tensor(spread[:, :], extremes_all[:, 0:HEADS], extremes_all[:, HEADS:2 * HEADS], ALU.add))
                link(dve.tensor_reduce(flag_f[:, :], spread[:, :], AX, ALU.max))
                link(dve.tensor_scalar(flag_f[:, :], flag_f[:, :], -1.0 if force_general else SAFE_RANGE, None, ALU.is_gt))
                link(dve.tensor_copy(flag[:, :], flag_f[:, :]), flag_made)
                flagged = dve.value_load(flag[0:1, 0:1], min_val=0, max_val=1)
                shift = adc[:, :, HEADS:2 * HEADS]
                with dve.If(flagged == 1):
                    if n == 0:
                        dve.tensor_copy(shift, src_score).then_inc(shift_made, 1)
                    else:
                        dve.memset(shift, -BIG).then_inc(shift_made, 1)
                    dve.wait_ge(shift_made, k + 1)
                    general_shift(k)
                with dve.Else():
                    dve.tensor_copy(shift, extremes_all[:, 0:HEADS].unsqueeze(1).to_broadcast([LANES, NT, HEADS])).then_inc(shift_made, 1)
                dve.nop()
                dve.wait_ge(shift_made, k + 1)
                link(dve.tensor_tensor(node4[:, :, :], shift, adc[:, :, 0:HEADS], ALU.add))
                link(dve.scalar_tensor_tensor(shift, node4[:, :, :], 0.2, node4[:, :, :], ALU.mult, ALU.max))

            def sums(n):
                kind, _, w = PASSES[n]

                def one_hots(T):
                    if T.has(1):
                        g, b = T.g(1), T.b(1)
                        dve.wait_ge(part_ready, n * STEPS + g * GS + GS)
                        dve.tensor_tensor(onehot[:, b, :, :],
                                          iota_f[:, :].unsqueeze(1).to_broadcast([LANES, GS, LANES]),
                                          dst_loc[:, bass.ds(g * GS, GS)].unsqueeze(2).to_broadcast([LANES, GS, LANES]),
                                          ALU.is_equal).then_inc(onehot_ready, 1)

                def add_parts(T):
                    if T.has(-1):
                        g = T.g(-1)
                        tile = registers(mybir.EngineType.DVE, node_tile[0:1, bass.ds(g * GS, GS)], NT - 1)
                        for k in range(GS):
                            s = n * STEPS + g * GS + k
                            dve.wait_ge(part_ready, s + NB * GS + 1)
                            dve.wait_ge(part_added, s + 4)
                            dst = acc[:, bass.ds(tile[k], 1), 0:w_add].rearrange("p o f -> p (o f)")
                            dve.tensor_tensor(dst, dst, ps_m[:, k % 4, 0:w_add], ALU.add).then_inc(part_added, 1)

                w_add = PASSES[n][1]

                def attend(T):
                    one_hots(T)
                    if T.has(0):
                        g, b, b2 = T.g(0), T.b(0), T.b(0, 2)
                        at = (ATTEND[n] * GROUPS + g) * 5
                        dst_scores = ps_a[:, b2, 0:2 * HEADS * GS].rearrange("p (k w) -> p k w", w=2 * HEADS)
                        dve.wait_ge(gathered[b], 16 * GS * (n * (GROUPS // NB) + T.before(0) + 1))
                        dve.wait_ge(dst_ready, ATTEND[n] * GROUPS + g + 3)
                        dve.tensor_tensor(score2[:, :, :], rows[:, b, :, D:D + HEADS], dst_scores[:, :, 0:HEADS], ALU.add).then_inc(score_chain, 1)
                        dve.wait_ge(score_chain, at + 1)
                        dve.scalar_tensor_tensor(score3[:, :, :], score2[:, :, :], 0.2, score2[:, :, :], ALU.mult, ALU.max).then_inc(score_chain, 1)
                        dve.wait_ge(score_chain, at + 2)
                        dve.tensor_tensor(score2[:, :, :], score3[:, :, :], dst_scores[:, :, HEADS:2 * HEADS], ALU.subtract).then_inc(score_chain, 1)
                        if n == 2:
                            outside = edge_w[:, bass.ds(g * GS, GS)].unsqueeze(2).to_broadcast([LANES, GS, HEADS])
                            dve.tensor_tensor(score3[:, :, :], score3[:, :, :], outside, ALU.add).then_inc(score_chain, 1)
                            dve.wait_ge(score_chain, at + 4)
                            dve.tensor_tensor(best[:, :, :], best[:, :, :], score3[:, :, :], ALU.max).then_inc(score_chain, 1)
                            dve.wait_ge(score_chain, at + 5)
                        else:
                            dve.sem_inc(score_chain, 2)
                            dve.wait_ge(score_chain, at + 5)
                        dve.tensor_scalar(score[:, :, :], score2[:, :, :], 0.0, None, ALU.min).then_inc(scored, 1)
                    add_parts(T)
                    if T.has(0):
                        dve.wait_ge(exp_ready, ATTEND[n] * GROUPS + g + 1)
                        msg = rows[:, b, :, 0:D].rearrange("p k (h c) -> p k h c", c=C)
                        dve.tensor_tensor(msg, msg, spread_heads(rows[:, b, :, D:D + HEADS], GS), ALU.mult).then_inc(msg_ready, 1)

                def edge_filter(T):
                    if T.has(0):
                        g, b = T.g(0), T.b(0)
                        dve.wait_ge(gathered[b], 16 * GS * (n * (GROUPS // NB) + T.before(0) + 1))
                        for k in range(GS):
                            if k % 4 == 0:
                                dve.wait_ge(layer2_ready, g * 2 + k // 4 + 3)
                            row = rows[:, b, k, 0:D]
                            ins = dve.scalar_tensor_tensor(row, ps_a[:, k // 4, LANES * (k % 4):LANES * (k % 4) + LANES],
                                                           edge_w[:, bass.ds(g * GS + k, 1)], row, ALU.mult, ALU.mult)
                        ins.then_inc(msg_ready, 1)
                    add_parts(T)
                    one_hots(T)
                    if T.has(1):
                        g = T.g(1)
                        for q in range(2):
                            dve.wait_ge(act_chain, g * 8 + 8 + 6 + q + 1)
                            dve.tensor_tensor(ssp_r[q], ssp_r[q], ssp_a[q], ALU.add).then_inc(ssp_ready, 1)

                def plain(T):
                    one_hots(T)
                    add_parts(T)

                over_groups(dve, {"attend": attend, "filter": edge_filter, "plain": plain}[kind])
                dve.wait_ge(part_added, (n + 1) * STEPS + 4)

            def norm(l):
                link(dve.tensor_reduce(stat[:, :], x[:, :, :], AX, ALU.add))
                link(dve.tensor_scalar(stat[:, :], stat[:, :], 1.0 / D, None, ALU.mult))
                link(dve.tensor_tensor(x[:, :, :], x[:, :, :], over_nodes(stat[:, :], D), ALU.subtract), centred)
                dve.wait_ge(squared, l + 1)
                link(dve.tensor_reduce(stat[:, :], feats, AX, ALU.add))
                link(dve.tensor_scalar(stat[:, :], stat[:, :], 1.0 / D, LN_EPS, ALU.mult, ALU.add), var_made)
                dve.wait_ge(root_made, l + 1)
                link(dve.reciprocal(stat2[:, :], stat[:, :]))
                link(dve.tensor_tensor(x[:, :, :], x[:, :, :], over_nodes(stat2[:, :], D), ALU.mult))

            def ask_product(m):
                dve.drain().then_inc(nm_from, 1)
                product(m)

            def over_sums(denominator):
                link(dve.reciprocal(node4[:, :, :], denominator))
                link(dve.tensor_tensor(heads(feats), heads(feats), spread_heads(node4[:, :, :], NT), ALU.mult))

            dve.wait_ge(consts_in, 16 * N_CONST)
            dve.wait_ge(x_in, 16)
            ask_product(0)
            table_ready(0)
            dve.wait_ge(tiles_in, 32)
            shifts(0)
            self_score = acc[:, :, D:D + HEADS]
            link(dve.tensor_tensor(node4[:, :, :], self_score, adc[:, :, 0:HEADS], ALU.add))
            link(dve.scalar_tensor_tensor(node4b[:, :, :], node4[:, :, :], 0.2, node4[:, :, :], ALU.mult, ALU.max))
            link(dve.tensor_tensor(node4[:, :, :], node4b[:, :, :], adc[:, :, HEADS:2 * HEADS], ALU.subtract), self_scored)
            dve.wait_ge(self_exp, 1)
            dve.tensor_tensor(heads(feats), heads(feats), spread_heads(self_score, NT), ALU.mult)
            link(dve.memset(acc[:, :, D + HEADS:D + HEADS + 1], 1.0))
            sums(0)
            dve.tensor_copy(degree[:, :].unsqueeze(2), acc[:, :, D + HEADS:D + HEADS + 1])
            link(dve.tensor_scalar(node4b[:, :, :], self_score, 1e-16, None, ALU.add))
            over_sums(node4b[:, :, :])
            link(dve.tensor_tensor(feats, feats, over_tiles(0, D), ALU.add), tanh_asked)
            dve.wait_ge(tanh_done, 1)
            link(dve.tensor_tensor(x[:, :, :], x[:, :, :], feats, ALU.add))
            norm(0)

            if layers > 1:
                ask_product(1)
                table_ready(1)
                sums(1)
                ask_product(2)
                link(dve.tensor_tensor(feats, feats, over_tiles(1, D), ALU.add), ssp_asked)
                for q in range(4):
                    dve.wait_ge(ssp_log, 3 * q + 3)
                    part = acc[:, 25 * q:25 * q + 25, 0:D]
                    link(dve.scalar_tensor_tensor(part, part, 0.0, ssp_tmp[q % 2], ALU.max, ALU.add), ssp_added)
                ask_product(3)
                link(dve.tensor_tensor(x[:, :, :], x[:, :, :], feats, ALU.add))
                link(dve.tensor_tensor(x[:, :, :], x[:, :, :], over_tiles(2, D), ALU.add))
                norm(1)

            if layers > 2:
                link(dve.tensor_scalar(work[:, 0:STEPS], dst_loc[:, :], -0.5, -BIG, ALU.is_lt, ALU.mult))
                link(dve.tensor_scalar(edge_w[:, :], dst_loc[:, :], LANES - 0.5, -BIG, ALU.is_gt, ALU.mult))
                link(dve.tensor_tensor(edge_w[:, :], edge_w[:, :], work[:, 0:STEPS], ALU.add))
                link(dve.memset(best[:, :, :], -BIG))
                ask_product(4)
                table_ready(2)
                shifts(2)
                link(dve.memset(acc[:, :, :], 0.0))
                sums(2)
                link(dve.tensor_reduce(best_all[:, 0:1], best[:, :, :].rearrange("p k h -> p (k h)"), AX, ALU.max), best_made)
                dve.wait_ge(best_reduced, 1)
                link(dve.tensor_scalar(node4[:, :, :], adc[:, :, HEADS:2 * HEADS], best_all[:, 1:2], -1.0, ALU.subtract, ALU.mult))
                link(dve.tensor_scalar(node4[:, :, :], node4[:, :, :], -LOG_1E16, 85.0, ALU.add, ALU.min), guard_asked)
                dve.wait_ge(guard_exp, 1)
                link(dve.tensor_tensor(node4b[:, :, :], node4b[:, :, :], self_score, ALU.add))
                link(dve.tensor_scalar(node4b[:, :, :], node4b[:, :, :], 1e-37, None, ALU.max))
                over_sums(node4b[:, :, :])
                link(dve.tensor_tensor(x[:, :, :], x[:, :, :], feats, ALU.add))
                link(dve.tensor_tensor(x[:, :, :], x[:, :, :], over_tiles(3, D), ALU.add))
                norm(2)

            if layers > 3:
                def rescale(w):
                    f = acc[:, :, 0:w]
                    link(dve.tensor_tensor(f, f, over_nodes(inv_root[:, :], w), ALU.mult))

                def add_bias(n, w):
                    f = acc[:, :, 0:w]
                    link(dve.tensor_tensor(f, f, over_tiles(n, w), ALU.add))

                def relu():
                    link(dve.tensor_scalar(feats, feats, 0.0, None, ALU.max))

                link(dve.tensor_copy(degree[:, :], degree[:, :]), degree_made)
                dve.wait_ge(degree_root, 1)
                link(dve.reciprocal(inv_root[:, :], inv_root[:, :]))
                ask_product(5)
                table_ready(3)
                sums(3)
                rescale(D)
                add_bias(4, D)
                relu()
                ask_product(6)
                table_ready(4)
                sums(4)
                rescale(HID)
                add_bias(5, HID)
                rescale(HID)
                table_ready(5)
                sums(5)
                rescale(HID)
                ask_product(7)
                add_bias(6, D)
                relu()
                ask_product(8)
                table_ready(6)
                sums(6)
                rescale(D)
                add_bias(7, D)
                link(dve.tensor_tensor(x[:, :, :], x[:, :, :], feats, ALU.add))
                norm(3)
            dve.drain().then_inc(out_ready, 1)


_OUT = (N_NODES, D)


def kernel(**inputs):
    import numpy as _np
    import concourse.bacc as _bacc
    from concourse import mybir as _mybir
    from concourse.bass_utils import run_bass_kernel_spmd as _run

    put = {k: _np.ascontiguousarray(v) for k, v in inputs.items()}
    lay = {}
    lay["x"] = _np.concatenate([put["x"], _np.zeros((NT * LANES - N_NODES, D), _np.float32)])
    spare = ET * LANES - N_EDGES
    lay["src"] = _np.concatenate([put["src"], _np.zeros(spare, _np.int32)])
    lay["dst"] = _np.concatenate([put["dst"], _np.full(spare, REAL_NT * LANES - 1, _np.int32)])
    lay["edge_weight"] = _np.concatenate([put["edge_weight"], _np.zeros(spare, _np.float32)])
    attr = _np.concatenate([put["edge_attr_50"], _np.zeros((spare, NF), _np.float32)])
    lay["edge_attr_t"] = attr.reshape(ET, LANES, NF).transpose(0, 2, 1)
    lay["L0_WT"], lay["L2_WT"] = put["L0_gnn_W"].T, put["L2_gnn_W_proj"].T
    lay["L1_mlp_w0T"], lay["L1_mlp_w2T"] = put["L1_gnn_mlp_w0"].T, put["L1_gnn_mlp_w2"].T
    lay["L1_lin1_wT"], lay["L1_lin2_wT"], lay["L1_lin_wT"] = (put["L1_gnn_lin1_w"].T, put["L1_gnn_lin2_w"].T, put["L1_gnn_lin_w"].T)
    for name in ("L0_gnn_att_src", "L0_gnn_att_dst", "L2_gnn_a_src", "L2_gnn_a_tgt"):
        lay[name] = put[name].reshape(-1)
    for name in ("L0_gnn_W", "L2_gnn_W_proj", "L3_gnn_W1", "L3_gnn_W2", "L3_gnn_W3", "L3_gnn_W4", "L1_gnn_mlp_b0", "L1_gnn_mlp_b2", *BIASES):
        lay[name] = put[name]

    nc = _bacc.Bacc("TRN2", target_bir_lowering=False, num_devices=1)
    arrays, args = {}, {}
    for name, v in lay.items():
        v = _np.ascontiguousarray(v)
        arrays[f"in_{name}_dram"] = v
        args[name] = nc.dram_tensor(f"in_{name}_dram", v.shape, _mybir.dt.from_np(v.dtype), kind="ExternalInput").ap()
    out = nc.dram_tensor("out_0_dram", _OUT, F32, kind="ExternalOutput").ap()
    build(nc, args, out)
    r = _run(nc, [arrays], core_ids=[0])
    return r.results[0]["out_0_dram"]
```
